# Optimizing a Trainium2 kernel written in Bass

```python
import numpy as np
import jax
import jax.numpy as jnp

def _softmax(x, axis=-1):
    return jax.nn.softmax(x, axis=axis)

def _gelu(x):
    return jax.nn.gelu(x, approximate=True)

def _silu(x):
    return jax.nn.silu(x)

def _sigmoid(x):
    return jax.nn.sigmoid(x)

def _layernorm(x, axis=-1, eps=1e-05):
    m = jnp.mean(x, axis=axis, keepdims=True)
    v = jnp.var(x, axis=axis, keepdims=True)
    return (x - m) / jnp.sqrt(v + eps)

def _scatter_add(tgt, idx, src, axis=0):
    return tgt.at[idx].add(src)

def _segment_sum(src, seg, n):
    return jax.ops.segment_sum(src, seg, n)
kernel_name = 'mk_gnn_resnorm_d1_gnn_r32_4ff6b8'

def setup_inputs(seed: int=0):
    np.random.seed(seed)
    _w = jnp.asarray

    def _rec_inputs():
        import jax
        import jax.numpy as jnp
        _gk = jax.random.key(seed)
        x = -0.000202 + 1 * jax.random.normal(jax.random.fold_in(_gk, 1), (3125, 128), jnp.float32)
        src = jax.random.randint(jax.random.fold_in(_gk, 2), (50000,), 0, 3125, jnp.int32)
        dst = jnp.minimum((3125 * jax.random.uniform(jax.random.fold_in(_gk, 3), (50000,)) ** 2.0).astype(jnp.int32), 99999)
        _o = jnp.argsort(dst, stable=True)
        src = src[_o]
        dst = dst[_o]
        return (x, src, dst)
    x, src, dst = _rec_inputs()

    def _L0_gnn_setup():
        import jax, jax.numpy as jnp
        import numpy as np
        N_NODES = 50000
        N_EDGES = 25000
        IN_DIM = 128
        HID = 128
        TIME = 6.0
        STEPS = 12
        key = jax.random.key(seed)
        ks = jax.random.split(key, 8)
        gat_out = jax.random.normal(ks[0], (N_NODES, IN_DIM), dtype=jnp.float32)
        edge_index = jax.random.randint(ks[1], (2, N_EDGES), 0, N_NODES, dtype=jnp.int64)
        W_in = jax.random.normal(ks[2], (IN_DIM, HID), dtype=jnp.float32) * (1.0 / np.sqrt(IN_DIM))
        b_in = jnp.zeros((HID,), dtype=jnp.float32)
        W1 = jax.random.normal(ks[3], (HID, 2 * HID), dtype=jnp.float32) * (1.0 / np.sqrt(HID))
        b1 = jnp.zeros((2 * HID,), dtype=jnp.float32)
        W2 = jax.random.normal(ks[4], (2 * HID, HID), dtype=jnp.float32) * (1.0 / np.sqrt(2 * HID))
        b2 = jnp.zeros((HID,), dtype=jnp.float32)
        clearance = jnp.full((1,), 0.1, dtype=jnp.float32)
        return {'gat_out': gat_out, 'edge_index': edge_index, 'W_in': W_in, 'b_in': b_in, 'W1': W1, 'b1': b1, 'W2': W2, 'b2': b2, 'clearance': clearance}
    _L0_gnn_all = _L0_gnn_setup()
    _L0_gnn_in = {k: v for k, v in _L0_gnn_all.items() if k in ('W_in', 'b_in', 'W1', 'b1', 'W2', 'b2', 'clearance')}
    del _L0_gnn_all
    return {'x': x, 'src': src, 'dst': dst, 'L0_gnn_W_in': _L0_gnn_in['W_in'], 'L0_gnn_b_in': _L0_gnn_in['b_in'], 'L0_gnn_W1': _L0_gnn_in['W1'], 'L0_gnn_b1': _L0_gnn_in['b1'], 'L0_gnn_W2': _L0_gnn_in['W2'], 'L0_gnn_b2': _L0_gnn_in['b2'], 'L0_gnn_clearance': _L0_gnn_in['clearance']}

def reference(x, src, dst, L0_gnn_W_in, L0_gnn_b_in, L0_gnn_W1, L0_gnn_b1, L0_gnn_W2, L0_gnn_b2, L0_gnn_clearance):
    import jax
    import jax.numpy as jnp

    def _L0_gnn_ref(gat_out, edge_index, W_in, b_in, W1, b1, W2, b2, clearance):
        import jax, jax.numpy as jnp
        import numpy as np
        N_NODES = 50000
        N_EDGES = 25000
        IN_DIM = 128
        HID = 128
        TIME = 6.0
        STEPS = 12
        N = gat_out.shape[0]
        dt = TIME / STEPS
        src, dst = (edge_index[0], edge_index[1])
        h = jnp.tanh(gat_out @ W_in + b_in)
        deg = jax.ops.segment_sum(jnp.ones((src.shape[0],), dtype=h.dtype), dst, num_segments=N)
        deg = jnp.clip(deg, 1.0, None)[:, None]
        decay = jax.nn.relu(clearance)

        def step(h, _):
            agg = jax.ops.segment_sum(h[src], dst, num_segments=N) / deg
            diff = jnp.tanh(jax.nn.gelu(agg @ W1 + b1, approximate=False) @ W2 + b2)
            h = h + (diff - decay * h) * dt
            return (h, None)
        h, _ = jax.lax.scan(step, h, None, length=STEPS)
        return h
    edge_index = jnp.stack([src, dst])
    x = _layernorm(x + _L0_gnn_ref(x, edge_index, L0_gnn_W_in, L0_gnn_b_in, L0_gnn_W1, L0_gnn_b1, L0_gnn_W2, L0_gnn_b2, L0_gnn_clearance), axis=-1)
    return x

_drawn_inputs = setup_inputs


def setup_inputs(seed=0):
    import zlib

    import numpy as np

    out = dict(_drawn_inputs(seed))
    spreads = {'L0_gnn_b_in': (0.0, 0.1), 'L0_gnn_b1': (0.0, 0.1), 'L0_gnn_b2': (0.0, 0.1)}
    factors = {}
    for name, (base, spread) in spreads.items():
        noise = np.random.default_rng([zlib.crc32(name.encode()), seed]).standard_normal(out[name].shape)
        drawn = base * np.exp(spread * noise) if base else spread * noise
        out[name] = jnp.asarray(drawn.astype(out[name].dtype))
    for name, factor in factors.items():
        out[name] = (out[name] * factor).astype(out[name].dtype)
    return out
```

```python
import concourse.bass as bass
from concourse import mybir
from contextlib import ExitStack


def gnn_resnorm(nc, x, src, dst, w_in, b_in, w1, b1, w2, b2, clearance, out):
    fp32, fp16, i32 = mybir.dt.float32, mybir.dt.float16, mybir.dt.int32
    ALU, ACT, AX = mybir.AluOpType, mybir.ActivationFunctionType, mybir.AxisListType

    NODES, D = x.shape
    EDGES = src.shape[0]
    HID2 = w1.shape[1]
    STEPS, DT, EPS = 12, 0.5, 1e-5
    TP, NT = 125, 25
    assert TP * NT == NODES and HID2 == 2 * D
    CHUNKS = [4, 4, 4, 4, 3, 3, 3]
    NC_ = len(CHUNKS)
    FIRST = [sum(CHUNKS[:j]) for j in range(NC_)]
    CHUNK_OF = [j for j, n in enumerate(CHUNKS) for _ in range(n)]
    GE = 125
    NG = EDGES // GE
    GQ, GI = 100, 4
    WD = 25
    NW = NODES // WD
    KEYS = NT * WD
    TA = 13
    KA, KB = TA * WD, (NT - TA) * WD
    RING = 4
    LOGS = 10
    ROUND = 1.5 * 2.0 ** 23

    x_tiles = x.rearrange("(t p) d -> p t d", p=TP)
    out_tiles = out.rearrange("(t p) d -> p t d", p=TP)

    ctx = ExitStack()
    with ctx:
        def sem(name):
            return ctx.enter_context(nc.semaphore(name))

        ARENA = 212800
        arena = ctx.enter_context(nc.sbuf_tensor("arena", [128, ARENA], mybir.dt.uint8))
        base_of_arena = nc.sbuf_base - ARENA

        class Region:
            def __init__(self, start, end):
                self.at, self.end = start, end

            def place(self, name, shape, dt):
                size = 1
                for n in shape[1:]:
                    size *= n
                size *= 2 if dt == fp16 else 4
                self.at = (self.at + 31) // 32 * 32
                t = nc.alloc_sbuf_tensor_at(name, shape, dt, offset=base_of_arena + self.at)
                self.at += size
                assert self.at <= self.end, (name, self.at, self.end)
                return t

        A_END = 156256
        H_END = A_END + 25600
        INV_END = H_END + 12512
        M_END = INV_END + 14144
        counts = Region(0, A_END).place("counts", [TP, NT, NODES], fp16)
        hparts = Region(A_END, H_END).place("hparts", [TP, 2, 2, NT * D], fp16)
        inv_degree = Region(H_END, INV_END).place("inv_degree", [D, NODES], fp32)
        keep = Region(M_END, ARENA)
        w1_sb = keep.place("w1_sb", [D, HID2], fp32)
        w2_sb = keep.place("w2_sb", [D, 2, D], fp32)
        b2_all = keep.place("b2_all", [TP, D], fp32)
        table_warm = keep.place("table_warm", [D, 2], fp32)
        b1_col = keep.place("b1_col", [D, 2], fp32)
        ones16 = keep.place("ones16", [TP, D], fp16)
        bound = keep.place("bound", [D, STEPS + 1], fp32)
        scale_bits = keep.place("scale_bits", [D, STEPS + 1], i32)
        rates = keep.place("rates", [D, 3, STEPS + 1], fp32)
        rates_now = keep.place("rates_now", [D, 2, 3], fp32)
        clear_in = keep.place("clear_in", [D, 1], fp32)
        decay_c = keep.place("decay_c", [D, 3], fp32)
        mlp = Region(INV_END, M_END)
        aggT = mlp.place("aggT", [D, 512], fp32)
        hidden = mlp.place("hidden", [D, 2, 500], fp32)
        diff = mlp.place("diff", [TP, 512], fp32)
        held = mlp.place("held", [TP, 512], fp32)
        x_sb = Region(INV_END, M_END).place("x_sb", [TP, NT, D], fp32)
        first = Region(H_END, INV_END)
        xT = first.place("xT", [D, 512], fp32)
        h0 = first.place("h0", [TP, 512], fp32)
        w_in_sb = first.place("w_in_sb", [D, D], fp32)
        b_in_row = first.place("b_in_row", [1, D], fp32)
        ones_row = first.place("ones_row", [1, D], fp32)
        build = Region(A_END + 12800, H_END)
        key_hot = build.place("key_hot", [GE, RING, KEYS], fp16)
        src_hot = build.place("src_hot", [GE, RING, TP], fp16)
        iota_key = build.place("iota_key", [GE, KEYS], fp16)
        iota_src = build.place("iota_src", [GE, TP], fp16)
        key = build.place("key", [GE, NG], fp32)
        src_key = build.place("src_key", [GE, NG], fp32)
        more = Region(first.at, INV_END)
        window_key = more.place("window_key", [GE, NW], fp32)
        table = more.place("table", [1, 3, NW], i32)
        prep = Region(0, A_END)
        dst_i = prep.place("dst_i", [GQ, GI * GE], i32)
        src_i = prep.place("src_i", [GQ, GI * GE], i32)
        dst_f = prep.place("dst_f", [GQ, GI * GE], fp32)
        src_f = prep.place("src_f", [GQ, GI * GE], fp32)
        extreme = prep.place("extreme", [GQ, 2, GI], fp32)
        extreme_diag = prep.place("extreme_diag", [GQ, 2, GI, GQ], fp32)
        ident = prep.place("ident", [128, 128], fp32)
        ones_f = prep.place("ones_f", [128, 128], fp32)
        upto = prep.place("upto", [NW, 2, NW], fp32)
        from_end = prep.place("from_end", [NW, GI, GQ], fp32)
        from_start = prep.place("from_start", [NW, GI, GQ], fp32)
        win_lo = prep.place("win_lo", [NW, 1], fp32)
        win_hi = prep.place("win_hi", [NW, 1], fp32)
        tmp = prep.place("tmp", [GE, 6, NG], fp32)
        span = prep.place("span", [NW, 4], fp32)

        norm = Region(0, A_END)
        x_last = norm.place("x_last", [TP, NT, D], fp32)[:, :, :]
        stats = norm.place("stats", [TP, NT, 6], fp32)
        meanvar = norm.place("meanvar", [TP, NT, 2], fp32)
        rstd = norm.place("rstd", [TP, NT], fp32)

        PS = ctx.enter_context(nc.psum_tensor("PS", [128, 8, 512], fp32))

        dst_loaded, src_loaded, x_loaded, weights_loaded = sem("dst_loaded"), sem("src_loaded"), sem("x_loaded"), sem("weights_loaded")
        consts_made = sem("consts_made")
        bounds_made = sem("bounds_made")
        gps_order = sem("gps_order")
        dve_order = sem("dve_order")
        rates_set = sem("rates_set")
        edges_f = sem("edges_f")
        diag_made = sem("diag_made")
        edges_T = sem("edges_T")
        extremes_B = sem("extremes_B")
        spans_made = sem("spans_made")
        table_rows = sem("table_rows")
        table_made = sem("table_made")
        xT_ps, xT_made, pre0_ps, h0_made, h_high, h_low = sem("xT_ps"), sem("xT_made"), sem("pre0_ps"), sem("h0_made"), sem("h_high"), sem("h_low")
        hot_free, hot_made, window_summed, window_free = sem("hot_free"), sem("hot_made"), sem("window_summed"), sem("window_free")
        degree_ps, degree_used = sem("degree_ps"), sem("degree_used")
        agg_ps, agg_made, z_ps, gelu_made = sem("agg_ps"), sem("agg_made"), sem("z_ps"), sem("gelu_made")
        pre_ps, pre_made, diff_made, held_made, h_made = sem("pre_ps"), sem("pre_made"), sem("diff_made"), sem("held_made"), sem("h_made")
        x_again, mean_var, std_made, out_made, out_stored = sem("x_again"), sem("mean_var"), sem("std_made"), sem("out_made"), sem("out_stored")

        N_CONST = 12
        block = ctx.enter_context(nc.Block())

        def cols(j):
            return slice(FIRST[j] * TP, (FIRST[j] + CHUNKS[j]) * TP)

        def feats(j):
            return slice(FIRST[j] * D, (FIRST[j] + CHUNKS[j]) * D)

        @block.sync
        def _(sp):
            sp.dma_start(dst_i[:, :], dst.rearrange("(q e) -> q e", q=GQ)).then_inc(dst_loaded, 16)
            sp.dma_start(src_i[:, :], src.rearrange("(q e) -> q e", q=GQ)).then_inc(src_loaded, 16)
            sp.dma_start(w_in_sb[:, :], w_in).then_inc(weights_loaded, 16)
            sp.dma_start(b_in_row[:, :], b_in.rearrange("(a n) -> a n", a=1)).then_inc(weights_loaded, 16)
            sp.dma_start(clear_in[:, :], clearance.partition_broadcast(D)).then_inc(weights_loaded, 16)
            sp.dma_start(w1_sb[:, :], w1).then_inc(weights_loaded, 16)
            sp.dma_start(w2_sb[:, :, :], w2.rearrange("(m k) n -> k m n", k=D)).then_inc(weights_loaded, 16)
            for m in range(2):
                sp.dma_start(b1_col[:, m:m + 1], b1[m * D:(m + 1) * D].rearrange("(k a) -> k a", a=1)).then_inc(weights_loaded, 16)
            sp.dma_start(b2_all[:, :], b2.partition_broadcast(TP)).then_inc(weights_loaded, 16)
            sp.dma_start(x_sb[:, :, :], x_tiles).then_inc(x_loaded, 16)
            sp.wait_ge(agg_ps, STEPS * NC_)
            sp.dma_start(x_last, x_tiles).then_inc(x_again, 16)
            for j in range(NC_):
                sp.wait_ge(out_made, j + 1)
                sp.dma_start(out_tiles[:, FIRST[j]:FIRST[j] + CHUNKS[j], :],
                             x_last[:, FIRST[j]:FIRST[j] + CHUNKS[j], :]).then_inc(out_stored, 16)
            sp.wait_ge(out_stored, 16 * NC_)

        N_WEIGHTS = 8 * 16
        @block.gpsimd
        def _(pool):
            ordered = [0]

            def link(ins):
                ordered[0] += 1
                ins.then_inc(gps_order, 1)
                pool.wait_ge(gps_order, ordered[0])

            link(nc.gpsimd.memset(ident[:, :], 0.0))
            nc.gpsimd.affine_select(out=ident[:, :], in_=ident[:, :], compare_op=ALU.not_equal, fill=1.0, base=0,
                                    pattern=[[-1, 128]], channel_multiplier=1).then_inc(consts_made, 1)
            nc.gpsimd.memset(ones_f[:, :], 1.0).then_inc(consts_made, 1)
            nc.gpsimd.memset(ones_row[:, :], 1.0).then_inc(consts_made, 1)
            nc.gpsimd.iota(from_end[:, :, :], pattern=[[-1, GI], [-GI, GQ]], base=NG, channel_multiplier=0,
                           allow_small_or_imprecise_dtypes=True).then_inc(consts_made, 1)
            nc.gpsimd.iota(from_start[:, :, :], pattern=[[1, GI], [GI, GQ]], base=1, channel_multiplier=0,
                           allow_small_or_imprecise_dtypes=True).then_inc(consts_made, 1)
            nc.gpsimd.iota(win_lo[:, :], pattern=[[0, 1]], base=0, channel_multiplier=WD,
                           allow_small_or_imprecise_dtypes=True).then_inc(consts_made, 1)
            nc.gpsimd.iota(win_hi[:, :], pattern=[[0, 1]], base=WD - 1, channel_multiplier=WD,
                           allow_small_or_imprecise_dtypes=True).then_inc(consts_made, 1)
            link(nc.gpsimd.memset(upto[:, :, :], 1.0))
            nc.gpsimd.affine_select(out=upto[:, :, :], in_=upto[:, :, :], compare_op=ALU.is_ge, fill=0.0, base=-1,
                                    pattern=[[1, 2], [1, NW]], channel_multiplier=-1).then_inc(consts_made, 1)
            nc.gpsimd.iota(iota_key[:, :], pattern=[[1, KEYS]], base=0, channel_multiplier=0,
                           allow_small_or_imprecise_dtypes=True).then_inc(consts_made, 1)
            nc.gpsimd.iota(iota_src[:, :], pattern=[[1, TP]], base=0, channel_multiplier=0,
                           allow_small_or_imprecise_dtypes=True).then_inc(consts_made, 1)
            nc.gpsimd.iota(window_key[:, :], pattern=[[128, NW]], base=0, channel_multiplier=0,
                           allow_small_or_imprecise_dtypes=True).then_inc(consts_made, 1)
            nc.gpsimd.memset(ones16[:, :], 1.0).then_inc(consts_made, 1)

            pool.wait_ge(weights_loaded, N_WEIGHTS)
            link(nc.gpsimd.tensor_scalar(decay_c[:, 0:1], clear_in[:, :], 0.0, None, ALU.max))
            link(nc.gpsimd.tensor_scalar(decay_c[:, 1:2], decay_c[:, 0:1], -DT, 1.0, ALU.mult, ALU.add))
            link(nc.gpsimd.tensor_scalar(decay_c[:, 2:3], decay_c[:, 1:2], -1.0, decay_c[:, 1:2], ALU.mult, ALU.max))
            link(nc.gpsimd.memset(bound[:, 0:1], 1.0))
            for k in range(STEPS):
                if k:
                    pool.wait_ge(bounds_made, k)
                nc.gpsimd.tensor_scalar(bound[:, k + 1:k + 2], bound[:, k:k + 1], decay_c[:, 2:3], DT,
                                        ALU.mult, ALU.add).then_inc(bounds_made, 1)

            for j, n in enumerate(CHUNKS):
                pool.wait_ge(h_high, j + 1)
                link(nc.gpsimd.tensor_scalar(h0[:, 0:n * D], h0[:, 0:n * D], 2.0 ** LOGS, None, ALU.mult))
                nc.gpsimd.tensor_tensor(hparts[:, 0, 1, feats(j)], h0[:, 0:n * D], hparts[:, 0, 0, feats(j)],
                                        ALU.subtract).then_inc(h_low, 1)

            with pool.Fori(0, STEPS // 2) as kk:
                for u in range(2):
                    pool.wait_ge(rates_set, kk * 2 + (u + 1))
                    for j, n in enumerate(CHUNKS):
                        pool.wait_ge(h_low, kk * (2 * NC_) + (u * NC_ + j + NC_))
                        nc.gpsimd.tensor_tensor(held[:, 0:n * D], hparts[:, u, 0, feats(j)], hparts[:, u, 1, feats(j)],
                                                ALU.add).then_inc(gps_order, 1)
                        pool.wait_ge(gps_order, kk * (2 * NC_) + (ordered[0] + u * NC_ + j + 1))
                        nc.gpsimd.tensor_tensor(held[:, 0:n * D], held[:, 0:n * D],
                                                rates_now[0:TP, u, 2:3].to_broadcast([TP, n * D]),
                                                ALU.mult).then_inc(held_made, 1)

        @block.scalar
        def _(act):
            act.wait_ge(weights_loaded, N_WEIGHTS)
            nc.scalar.activation(table_warm[:, :], b1_col[:, :], ACT.Gelu)
            for j, n in enumerate(CHUNKS):
                act.wait_ge(xT_ps, j + 1)
                nc.scalar.activation(xT[:, 0:n * TP], PS[:, 5, 0:n * TP], ACT.Copy).then_inc(xT_made, 1)
                act.wait_ge(pre0_ps, j + 1)
                if j:
                    act.wait_ge(h_low, j)
                nc.scalar.activation(h0[:, 0:n * D], PS[0:TP, 6, 0:n * D], ACT.Tanh).then_inc(h0_made, 1)
                act.wait_ge(h0_made, j + 1)
                nc.scalar.activation(hparts[:, 0, 0, feats(j)], h0[:, 0:n * D], ACT.Copy,
                                     scale=2.0 ** LOGS).then_inc(h_high, 1)

            act.sem_inc(window_free, 2)
            with act.Fori(0, NW) as w:
                act.wait_ge(window_summed, w + 1)
                nc.scalar.activation(counts[:, 0:TA, bass.ds(w * WD, WD)],
                                     PS[0:TP, bass.ds((w % 2) * 2, 1), 0:KA].rearrange("p a (t d) -> p (a t) d", d=WD),
                                     ACT.Copy)
                nc.scalar.activation(counts[:, TA:NT, bass.ds(w * WD, WD)],
                                     PS[0:TP, bass.ds((w % 2) * 2 + 1, 1), 0:KB].rearrange("p a (t d) -> p (a t) d", d=WD),
                                     ACT.Copy).then_inc(window_free, 1)

            with act.Fori(0, STEPS // 2) as kk:
                for u in range(2):
                    for j, n in enumerate(CHUNKS):
                        g = kk * (2 * NC_) + (u * NC_ + j)
                        for m in range(2):
                            act.wait_ge(z_ps, g * 2 + (m + 1))
                            nc.scalar.activation(hidden[:, m, 0:n * TP], PS[:, 2 + m, 0:n * TP], ACT.Gelu,
                                                 bias=b1_col[:, m:m + 1], scale=1.0).then_inc(gelu_made, 1)
                        act.wait_ge(pre_made, g + 1)
                        nc.scalar.activation(diff[:, 0:n * D], diff[:, 0:n * D], ACT.Tanh).then_inc(diff_made, 1)
                        act.wait_ge(h_made, g + 1)
                        nc.scalar.activation(hparts[:, 1 - u, 0, feats(j)], diff[:, 0:n * D], ACT.Copy).then_inc(h_high, 1)
            act.wait_ge(mean_var, 1)
            nc.scalar.activation(rstd[:, :], meanvar[:, :, 1], ACT.Sqrt, bias=0.0, scale=1.0).then_inc(std_made, 1)

        @block.vector
        def _(dve):
            ordered = [0]

            def link(ins):
                ordered[0] += 1
                ins.then_inc(dve_order, 1)
                dve.wait_ge(dve_order, ordered[0])

            dve.wait_ge(consts_made, N_CONST)
            dve.wait_ge(dst_loaded, 16)
            link(nc.vector.tensor_copy(dst_f[:, :], dst_i[:, :]))
            dve.wait_ge(src_loaded, 16)
            nc.vector.tensor_copy(src_f[:, :], src_i[:, :]).then_inc(edges_f, 1)
            by_group = dst_f[:, :].rearrange("q (i e) -> q i e", i=GI)
            nc.vector.tensor_reduce(extreme[:, 0, :], by_group, axis=AX.X, op=ALU.max)
            link(nc.vector.tensor_reduce(extreme[:, 1, :], by_group, axis=AX.X, op=ALU.min))
            for m in range(2):
                last = nc.vector.tensor_tensor(extreme_diag[:, m, :, :],
                                               ident[0:GQ, 0:GQ].unsqueeze(1).to_broadcast([GQ, GI, GQ]),
                                               extreme[:, m, :].unsqueeze(2).to_broadcast([GQ, GI, GQ]), ALU.mult)
            last.then_inc(diag_made, 1)
            dve.wait_ge(edges_T, 2)
            src_T = PS[0:GE, 0, 0:NG]
            dst_T = PS[0:GE, 1, 0:NG]
            q_src, q_dst, r_src, r_dst = (tmp[:, n, :] for n in range(4))
            nc.vector.tensor_scalar(q_src, src_T, -float(TP // 2), 1.0 / TP, ALU.add, ALU.mult)
            link(nc.vector.tensor_scalar(q_dst, dst_T, -float(WD // 2), 1.0 / WD, ALU.add, ALU.mult))
            link(nc.vector.tensor_scalar(tmp[:, 0:2, :], tmp[:, 0:2, :], ROUND, None, ALU.add))
            link(nc.vector.tensor_scalar(tmp[:, 0:2, :], tmp[:, 0:2, :], -ROUND, None, ALU.add))
            nc.vector.scalar_tensor_tensor(out=r_src, in0=q_src, scalar=-float(TP), in1=src_T, op0=ALU.mult, op1=ALU.add)
            link(nc.vector.scalar_tensor_tensor(out=r_dst, in0=q_dst, scalar=-float(WD), in1=dst_T, op0=ALU.mult, op1=ALU.add))
            by_i = lambda ap: ap.rearrange("p (i q) -> p i q", i=GI)
            as_i = lambda ap: ap.rearrange("p (q i) -> p i q", i=GI)
            nc.vector.scalar_tensor_tensor(out=as_i(key[:, :]), in0=by_i(q_src), scalar=float(WD), in1=by_i(r_dst),
                                           op0=ALU.mult, op1=ALU.add)
            link(nc.vector.scalar_tensor_tensor(out=as_i(src_key[:, :]), in0=by_i(q_dst), scalar=128.0, in1=by_i(r_src),
                                                op0=ALU.mult, op1=ALU.add))
            dve.wait_ge(extremes_B, 2)
            flat = lambda ap: ap.rearrange("p i q -> p (i q)")
            nc.vector.scalar_tensor_tensor(out=tmp[:, 4, :], in0=PS[0:NW, 2, 0:NG], scalar=win_lo[:, :], in1=flat(from_end[:, :, :]),
                                           op0=ALU.is_ge, op1=ALU.mult)
            link(nc.vector.scalar_tensor_tensor(out=tmp[:, 5, :], in0=PS[0:NW, 3, 0:NG], scalar=win_hi[:, :], in1=flat(from_start[:, :, :]),
                                                op0=ALU.is_le, op1=ALU.mult))
            link(nc.vector.tensor_reduce(span[:, 0:2], tmp[:, 4:6, :], axis=AX.X, op=ALU.max))
            link(nc.vector.tensor_scalar(span[:, 0:1], span[:, 0:1], -1.0, float(NG), ALU.mult, ALU.add))
            link(nc.vector.tensor_scalar(span[:, 0:1], span[:, 0:1], float(NG - 1), None, ALU.min))
            link(nc.vector.tensor_scalar(span[:, 2:3], span[:, 0:1], 1.0, None, ALU.add))
            link(nc.vector.tensor_tensor(span[:, 1:2], span[:, 1:2], span[:, 2:3], ALU.max))
            nc.vector.tensor_tensor(span[:, 3:4], span[:, 1:2], span[:, 0:1], ALU.subtract).then_inc(spans_made, 1)
            dve.wait_ge(table_rows, 1)
            rows = PS[0:1, 4, 0:3 * NW].rearrange("p (r w) -> p r w", w=NW)
            nc.vector.tensor_copy(table[:, 0:2, :], rows[:, 0:2, :])
            link(nc.vector.tensor_copy(table[:, 2, :], rows[:, 2, :]))
            nc.vector.tensor_tensor(table[:, 2, :], rows[:, 2, :], table[:, 0, :], ALU.subtract).then_inc(table_made, 1)

            dve.wait_ge(bounds_made, STEPS)
            link(nc.vector.tensor_scalar(scale_bits[:, :], bound[:, :].bitcast(i32), 0x7F800000, None, ALU.bitwise_and))
            link(nc.vector.tensor_scalar(rates[:, 0, :], scale_bits[:, :].bitcast(fp32), 2.0 ** -LOGS, None, ALU.mult))
            link(nc.vector.tensor_scalar(scale_bits[:, :], scale_bits[:, :], -1.0, float((2 * 127 + LOGS) << 23), ALU.mult, ALU.add))
            scale = scale_bits[:, :].bitcast(fp32)
            nc.vector.tensor_scalar(rates[:, 1, 0:STEPS], scale[:, 1:STEPS + 1], DT, None, ALU.mult)
            nc.vector.scalar_tensor_tensor(out=rates[:, 2, 0:STEPS], in0=scale[:, 1:STEPS + 1], scalar=decay_c[:, 1:2],
                                           in1=rates[:, 0, 0:STEPS], op0=ALU.mult, op1=ALU.mult).then_inc(hot_free, RING)

            dve.wait_ge(table_made, 1)
            with dve.Fori(0, NW) as w:
                p0 = dve.value_load(table[0:1, 0, bass.ds(w, 1)], min_val=0, max_val=NG * NW)
                p1 = dve.value_load(table[0:1, 1, bass.ds(w, 1)], min_val=0, max_val=NG * NW)
                off = dve.value_load(table[0:1, 2, bass.ds(w, 1)])
                with dve.Fori(p0, p1) as pair:
                    group = dve.snap(pair + off, min_val=0, max_val=NG - 1)
                    slot = dve.snap(pair % RING)
                    dve.wait_ge(hot_free, pair + 1)
                    nc.vector.tensor_scalar(key_hot[:, bass.ds(slot, 1), :].rearrange("p a k -> p (a k)"), iota_key[:, :],
                                            key[:, bass.ds(group, 1)], None, ALU.is_equal)
                    nc.vector.tensor_scalar(src_hot[:, bass.ds(slot, 1), :].rearrange("p a k -> p (a k)"), iota_src[:, :],
                                            window_key[:, bass.ds(w, 1)], src_key[:, bass.ds(group, 1)],
                                            ALU.add, ALU.is_equal).then_inc(hot_made, 1)

            dve.wait_ge(h_low, NC_)
            for j in range(NC_):
                dve.wait_ge(degree_ps, j + 1)
                n = CHUNKS[j] * TP
                link(nc.vector.tensor_scalar(inv_degree[:, cols(j)], PS[:, 5 + j % 2, 0:n], 1.0, None, ALU.max))
                nc.vector.reciprocal(inv_degree[:, cols(j)], inv_degree[:, cols(j)]).then_inc(degree_used, 1)
            dve.wait_ge(degree_used, NC_)

            b2_rep = lambda n: b2_all[:, :].unsqueeze(1).to_broadcast([TP, n, D])
            with dve.Fori(0, STEPS // 2) as kk:
                for u in range(2):
                    nc.vector.tensor_copy(rates_now[:, u, :], rates[:, :, bass.ds(kk * 2 + u, 1)].rearrange("p r k -> p (r k)"))\
                        .then_inc(rates_set, 1)
                    dve.wait_ge(rates_set, kk * 2 + (u + 1))
                    for j, n in enumerate(CHUNKS):
                        g = kk * (2 * NC_) + (u * NC_ + j)
                        N = n * TP
                        dve.wait_ge(agg_ps, g + 1)
                        nc.vector.scalar_tensor_tensor(out=aggT[:, 0:N], in0=PS[:, (u * NC_ + j) % 2, 0:N],
                                                       scalar=rates_now[:, u, 0:1], in1=inv_degree[:, cols(j)],
                                                       op0=ALU.mult, op1=ALU.mult).then_inc(agg_made, 1)
                        dve.wait_ge(pre_ps, g + 1)
                        nc.vector.tensor_tensor(diff[:, 0:n * D].rearrange("p (t d) -> p t d", d=D),
                                                PS[0:TP, 4, 0:n * D].rearrange("p (t d) -> p t d", d=D), b2_rep(n),
                                                ALU.add).then_inc(pre_made, 1)
                        dve.wait_ge(diff_made, g + 1)
                        dve.wait_ge(held_made, g + 1)
                        nc.vector.scalar_tensor_tensor(out=diff[:, 0:n * D], in0=diff[:, 0:n * D],
                                                       scalar=rates_now[0:TP, u, 1:2], in1=held[:, 0:n * D],
                                                       op0=ALU.mult, op1=ALU.add).then_inc(h_made, 1)
                        dve.wait_ge(h_made, g + 1)
                        dve.wait_ge(h_high, g + (NC_ + 1))
                        nc.vector.tensor_tensor(hparts[:, 1 - u, 1, feats(j)], diff[:, 0:n * D], hparts[:, 1 - u, 0, feats(j)],
                                                ALU.subtract).then_inc(h_low, 1)

            dve.wait_ge(x_again, 16)
            dve.wait_ge(h_low, (STEPS + 1) * NC_)
            xf = x_last.rearrange("p t d -> p (t d)")
            for part in range(2):
                link(nc.vector.scalar_tensor_tensor(out=xf, in0=hparts[:, 0, part, :], scalar=rates[0:TP, 0, STEPS:STEPS + 1],
                                                    in1=xf, op0=ALU.mult, op1=ALU.add))
            for t in range(NT):
                last = nc.vector.bn_stats(stats[:, t, :], x_last[:, t, :])
            link(last)
            for t in range(NT):
                last = nc.vector.bn_aggr(meanvar[:, t, :], stats[:, t, :])
            link(last)
            nc.vector.tensor_scalar(meanvar[:, :, 1], meanvar[:, :, 1], EPS, None, ALU.add).then_inc(mean_var, 1)
            dve.wait_ge(std_made, 1)
            link(nc.vector.reciprocal(rstd[:, :], rstd[:, :]))
            for j in range(NC_):
                for t in range(FIRST[j], FIRST[j] + CHUNKS[j]):
                    last = nc.vector.tensor_scalar(x_last[:, t, :], x_last[:, t, :], meanvar[:, t, 0:1], rstd[:, t:t + 1],
                                                   ALU.subtract, ALU.mult)
                last.then_inc(out_made, 1)

        @block.tensor
        def _(pe):
            pe.wait_ge(consts_made, N_CONST)
            pe.wait_ge(edges_f, 1)
            for m, lst in enumerate((src_f, dst_f)):
                for i in range(GI):
                    last = nc.tensor.transpose(PS[0:GE, m, i * GQ:(i + 1) * GQ], lst[:, i * GE:(i + 1) * GE], ident[0:GQ, 0:GQ])
                last.then_inc(edges_T, 1)
            pe.wait_ge(diag_made, 1)
            for m in range(2):
                nc.tensor.matmul(PS[0:NW, 2 + m, 0:NG], ones_f[0:GQ, 0:NW], extreme_diag[:, m, :, :].rearrange("p i q -> p (i q)"),
                                 start=True, stop=True).then_inc(extremes_B, 1)
            pe.wait_ge(x_loaded, 16)
            pe.wait_ge(weights_loaded, N_WEIGHTS)

            def table_matmuls():
                pe.wait_ge(spans_made, 1)
                nc.tensor.matmul(PS[0:1, 4, 0:NW], span[:, 3:4], upto[:, 0, :], start=True, stop=True)
                nc.tensor.matmul(PS[0:1, 4, NW:2 * NW], span[:, 3:4], upto[:, 1, :], start=True, stop=True)
                nc.tensor.matmul(PS[0:1, 4, 2 * NW:3 * NW], span[:, 0:1], ident[0:NW, 0:NW], start=True, stop=True)\
                    .then_inc(table_rows, 1)

            for j, n in enumerate(CHUNKS):
                for i in range(n):
                    last = nc.tensor.transpose(PS[:, 5, i * TP:(i + 1) * TP], x_sb[:, FIRST[j] + i, :], ident[0:TP, 0:TP])
                last.then_inc(xT_ps, 1)
                pe.wait_ge(xT_made, j + 1)
                if j:
                    pe.wait_ge(h0_made, j)
                for i in range(n):
                    nc.tensor.matmul(PS[0:TP, 6, i * D:(i + 1) * D], xT[:, i * TP:(i + 1) * TP], w_in_sb[:, :], start=True, stop=False)
                    last = nc.tensor.matmul(PS[0:TP, 6, i * D:(i + 1) * D], ones_row[:, 0:TP], b_in_row[:, :], start=False, stop=True)
                last.then_inc(pre0_ps, 1)
                if j == 1:
                    table_matmuls()

            pe.wait_ge(table_made, 1)
            with pe.Fori(0, NW) as w:
                p0 = pe.value_load(table[0:1, 0, bass.ds(w, 1)], min_val=0, max_val=NG * NW)
                p1 = pe.value_load(table[0:1, 1, bass.ds(w, 1)], min_val=0, max_val=NG * NW)
                bank = pe.snap((w % 2) * 2)
                pe.wait_ge(window_free, w + 1)
                for b in range(2):
                    nc.tensor.matmul(PS[0:TP, bass.ds(bank + b, 1), 511:512].rearrange("p a k -> p (a k)"), ones16[:, 0:TP],
                                     ones16[:, 0:1], start=True, stop=False, skip_group_check=True)
                with pe.Fori(p0, p1) as pair:
                    slot = pe.snap(pair % RING)
                    pe.wait_ge(hot_made, pair + 1)
                    hot = src_hot[:, bass.ds(slot, 1), :].rearrange("p a k -> p (a k)")
                    nc.tensor.matmul(PS[0:TP, bass.ds(bank, 1), 0:KA].rearrange("p a k -> p (a k)"), hot,
                                     key_hot[:, bass.ds(slot, 1), 0:KA].rearrange("p a k -> p (a k)"),
                                     start=False, stop=False, skip_group_check=True)
                    nc.tensor.matmul(PS[0:TP, bass.ds(bank + 1, 1), 0:KB].rearrange("p a k -> p (a k)"), hot,
                                     key_hot[:, bass.ds(slot, 1), KA:KEYS].rearrange("p a k -> p (a k)"),
                                     start=False, stop=False, skip_group_check=True).then_inc(hot_free, 1)
                for b in range(2):
                    last = nc.tensor.matmul(PS[0:TP, bass.ds(bank + b, 1), 511:512].rearrange("p a k -> p (a k)"), ones16[:, 0:TP],
                                            ones16[:, 0:1], start=False, stop=True, skip_group_check=True)
                last.then_inc(window_summed, 1)

            pe.wait_ge(window_free, NW + 2)
            for j in range(NC_):
                if j >= 2:
                    pe.wait_ge(degree_used, j - 1)
                for t in range(NT):
                    last = nc.tensor.matmul(PS[:, 5 + j % 2, 0:CHUNKS[j] * TP], ones16[:, :], counts[:, t, cols(j)],
                                            start=(t == 0), stop=(t == NT - 1))
                last.then_inc(degree_ps, 1)

            def aggregate(g, u, j, lo, hi):
                N = CHUNKS[j] * TP
                for q in range(lo, hi):
                    t, part = q // 2, q % 2
                    if j == 0 and part == 0 and t in FIRST:
                        pe.wait_ge(h_low, g + (CHUNK_OF[t] + 1))
                    last = nc.tensor.matmul(PS[:, (u * NC_ + j) % 2, 0:N], hparts[:, u, part, t * D:(t + 1) * D], counts[:, t, cols(j)],
                                            start=(q == 0), stop=(q == 2 * NT - 1))
                if hi == 2 * NT:
                    last.then_inc(agg_ps, 1)

            def layer1(g, j):
                N = CHUNKS[j] * TP
                pe.wait_ge(agg_made, g + 1)
                for m in range(2):
                    nc.tensor.matmul(PS[:, 2 + m, 0:N], w1_sb[:, m * D:(m + 1) * D], aggT[:, 0:N], start=True, stop=True)\
                        .then_inc(z_ps, 1)

            def layer2(g, j):
                pe.wait_ge(gelu_made, g * 2 + 2)
                for i in range(CHUNKS[j]):
                    for m in range(2):
                        last = nc.tensor.matmul(PS[0:TP, 4, i * D:(i + 1) * D], hidden[:, m, i * TP:(i + 1) * TP], w2_sb[:, m, :],
                                                start=(m == 0), stop=(m == 1))
                last.then_inc(pre_ps, 1)

            def chunk(g, r):
                u, j = r // NC_ % 2, r % NC_
                aggregate(g, u, j, 0, 6)
                layer1(g - 1, (j - 1) % NC_)
                aggregate(g, u, j, 6, 24)
                layer2(g - 1, (j - 1) % NC_)
                aggregate(g, u, j, 24, 2 * NT)

            aggregate(0, 0, 0, 0, 2 * NT)
            with pe.Fori(0, STEPS // 2 - 1) as kk:
                for r in range(1, 2 * NC_ + 1):
                    chunk(kk * (2 * NC_) + r, r)
            for r in range(1, 2 * NC_):
                chunk((STEPS - 2) * NC_ + r, r)
            layer1(STEPS * NC_ - 1, NC_ - 1)
            layer2(STEPS * NC_ - 1, NC_ - 1)


_INS = ["x", "src", "dst", "L0_gnn_W_in", "L0_gnn_b_in", "L0_gnn_W1", "L0_gnn_b1", "L0_gnn_W2", "L0_gnn_b2", "L0_gnn_clearance"]


def kernel(**inputs):
    import numpy as _np
    import concourse.bacc as _bacc
    from concourse import mybir as _mybir
    from concourse.bass_utils import run_bass_kernel_spmd as _run

    nc = _bacc.Bacc("TRN2", target_bir_lowering=False, num_devices=1)
    arrays, args = {}, []
    for name in _INS:
        a = _np.ascontiguousarray(inputs[name])
        arrays[f"in_{name}"] = a
        args.append(nc.dram_tensor(f"in_{name}", a.shape, _mybir.dt.from_np(a.dtype), kind="ExternalInput").ap())
    out = nc.dram_tensor("out_dram", inputs["x"].shape, _mybir.dt.float32, kind="ExternalOutput").ap()
    gnn_resnorm(nc, *args, out)
    r = _run(nc, [arrays], core_ids=[0])
    return r.results[0]["out_dram"]
```
